# Optimizing a Trainium2 kernel written in Bass

```python
import numpy as np
import jax
import jax.numpy as jnp

def _softmax(x, axis=-1):
    return jax.nn.softmax(x, axis=axis)

def _gelu(x):
    return jax.nn.gelu(x, approximate=True)

def _silu(x):
    return jax.nn.silu(x)

def _sigmoid(x):
    return jax.nn.sigmoid(x)

def _layernorm(x, axis=-1, eps=1e-05):
    m = jnp.mean(x, axis=axis, keepdims=True)
    v = jnp.var(x, axis=axis, keepdims=True)
    return (x - m) / jnp.sqrt(v + eps)

def _scatter_add(tgt, idx, src, axis=0):
    return tgt.at[idx].add(src)

def _segment_sum(src, seg, n):
    return jax.ops.segment_sum(src, seg, n)
kernel_name = 'mk_adj_resnorm_d4_adj_r2_1175f2'

def setup_inputs(seed: int=0):
    np.random.seed(seed)
    _w = jnp.asarray

    def _rec_inputs():
        import jax
        import jax.numpy as jnp
        _gk = jax.random.key(seed)
        x = -0.000929 + 1 * jax.random.normal(jax.random.fold_in(_gk, 1), (4096, 128), jnp.float32)
        _a = jax.random.bernoulli(jax.random.fold_in(_gk, 2), 0.000488281, (4096, 4096))
        _a = jnp.logical_or(_a, jnp.eye(4096, dtype=bool))
        _af = _a.astype(jnp.float32)
        _af = _af * jax.random.uniform(jax.random.fold_in(_gk, 3), (4096, 4096), jnp.float32, 0.05, 1)
        adj = _af
        return (x, adj)
    x, adj = _rec_inputs()

    def _L0_gnn_setup():
        import jax, jax.numpy as jnp
        import numpy as np
        N = 4096
        H = 128
        key = jax.random.key(seed)
        k_x, k_A, k_W = jax.random.split(key, 3)
        x = jax.random.normal(k_x, (N, H), dtype=jnp.float32)
        A = jax.random.uniform(k_A, (N, N), dtype=jnp.float32)
        alpha = jnp.array([0.5], dtype=jnp.float32)
        bound = 1.0 / np.sqrt(H)
        W = jax.random.uniform(k_W, (H, H), dtype=jnp.float32, minval=-bound, maxval=bound)
        b = jnp.zeros((H,), dtype=jnp.float32)
        t = jnp.zeros((1,), dtype=jnp.float32)
        return {'t': t, 'x': x, 'A': A, 'alpha': alpha, 'W': W, 'b': b}
    _L0_gnn_all = _L0_gnn_setup()
    _L0_gnn_in = {k: v for k, v in _L0_gnn_all.items() if k in ('t', 'alpha', 'W', 'b')}
    del _L0_gnn_all

    def _L1_gnn_setup():
        import jax, jax.numpy as jnp
        import numpy as np
        key = jax.random.key(seed)
        k1, k2, k3, k4 = jax.random.split(key, 4)
        n, in_dim, out_dim = (8192, 128, 128)
        h = jax.random.normal(k1, (n, in_dim), dtype=jnp.float32)
        adj = jax.random.uniform(k2, (n, n), dtype=jnp.float32)
        W_self = jax.random.normal(k3, (in_dim, out_dim), dtype=jnp.float32) * (1.0 / np.sqrt(in_dim))
        W_neigh = jax.random.normal(k4, (in_dim, out_dim), dtype=jnp.float32) * (1.0 / np.sqrt(in_dim))
        return {'h': h, 'adj': adj, 'W_self': W_self, 'W_neigh': W_neigh}
    _L1_gnn_all = _L1_gnn_setup()
    _L1_gnn_in = {k: v for k, v in _L1_gnn_all.items() if k in ('W_self', 'W_neigh')}
    del _L1_gnn_all

    def _L2_gnn_setup():
        import jax, jax.numpy as jnp
        import numpy as np
        NEG_SLOPE = 0.01
        N_U, N_V = (4096, 4096)
        U_F, V_F = (128, 128)
        HIDS = [128, 128]
        NUM_ROUNDS = 3

        def _glorot(key, fan_in, fan_out):
            lim = np.sqrt(6.0 / (fan_in + fan_out)).astype(np.float32)
            return jax.random.uniform(key, (fan_in, fan_out), jnp.float32, -lim, lim)

        def _mlp(x, W1, b1, W2, b2, W3, b3):
            a = jax.nn.leaky_relu
            x = a(x @ W1 + b1, NEG_SLOPE)
            x = a(x @ W2 + b2, NEG_SLOPE)
            return a(x @ W3 + b3, NEG_SLOPE)
        key = jax.random.key(seed)
        ks = jax.random.split(key, 12)
        inp = {'u_node_feats': jax.random.normal(ks[0], (N_U, U_F), jnp.float32), 'v_node_feats': jax.random.normal(ks[1], (N_V, V_F), jnp.float32), 'uv_adj_mat': jax.random.uniform(ks[2], (N_V, N_U), jnp.float32), 'vu_adj_mat': jax.random.uniform(ks[3], (N_U, N_V), jnp.float32)}
        dims_uv = [U_F] + HIDS + [V_F]
        dims_vu = [V_F] + HIDS + [U_F]
        k = 4
        for tag, dims in (('uv', dims_uv), ('vu', dims_vu)):
            for i in range(3):
                inp[f'{tag}_W{i + 1}'] = _glorot(ks[k], dims[i], dims[i + 1])
                k += 1
                inp[f'{tag}_b{i + 1}'] = jnp.zeros((dims[i + 1],), jnp.float32)
        return inp
    _L2_gnn_all = _L2_gnn_setup()
    _L2_gnn_in = {k: v for k, v in _L2_gnn_all.items() if k in ('v_node_feats', 'uv_W1', 'uv_b1', 'uv_W2', 'uv_b2', 'uv_W3', 'uv_b3', 'vu_W1', 'vu_b1', 'vu_W2', 'vu_b2', 'vu_W3', 'vu_b3')}
    del _L2_gnn_all

    def _L3_gnn_setup():
        import jax, jax.numpy as jnp
        import numpy as np
        N = 8192
        IN_DIM = 128
        OUT_DIM = 128

        def _message(X, A, W):
            deg = jnp.sum(A, axis=1, keepdims=True)
            A_norm = A / jnp.where(deg > 0, deg, 1.0)
            return A_norm @ X @ W
        key = jax.random.key(seed)
        k1, k2, k3, k4 = jax.random.split(key, 4)
        X = jax.random.normal(k1, (N, IN_DIM), dtype=jnp.float32)
        A = jax.random.uniform(k2, (N, N), dtype=jnp.float32)
        W_in = jax.random.normal(k3, (IN_DIM, OUT_DIM), dtype=jnp.float32) / np.sqrt(IN_DIM)
        W_out = jax.random.normal(k4, (IN_DIM, OUT_DIM), dtype=jnp.float32) / np.sqrt(IN_DIM)
        return {'X': X, 'A': A, 'W_in': W_in, 'W_out': W_out}
    _L3_gnn_all = _L3_gnn_setup()
    _L3_gnn_in = {k: v for k, v in _L3_gnn_all.items() if k in ('W_in', 'W_out')}
    del _L3_gnn_all
    return {'x': x, 'adj': adj, 'L0_gnn_t': _L0_gnn_in['t'], 'L0_gnn_alpha': _L0_gnn_in['alpha'], 'L0_gnn_W': _L0_gnn_in['W'], 'L0_gnn_b': _L0_gnn_in['b'], 'L1_gnn_W_self': _L1_gnn_in['W_self'], 'L1_gnn_W_neigh': _L1_gnn_in['W_neigh'], 'L2_gnn_v_node_feats': _L2_gnn_in['v_node_feats'], 'L2_gnn_uv_W1': _L2_gnn_in['uv_W1'], 'L2_gnn_uv_b1': _L2_gnn_in['uv_b1'], 'L2_gnn_uv_W2': _L2_gnn_in['uv_W2'], 'L2_gnn_uv_b2': _L2_gnn_in['uv_b2'], 'L2_gnn_uv_W3': _L2_gnn_in['uv_W3'], 'L2_gnn_uv_b3': _L2_gnn_in['uv_b3'], 'L2_gnn_vu_W1': _L2_gnn_in['vu_W1'], 'L2_gnn_vu_b1': _L2_gnn_in['vu_b1'], 'L2_gnn_vu_W2': _L2_gnn_in['vu_W2'], 'L2_gnn_vu_b2': _L2_gnn_in['vu_b2'], 'L2_gnn_vu_W3': _L2_gnn_in['vu_W3'], 'L2_gnn_vu_b3': _L2_gnn_in['vu_b3'], 'L3_gnn_W_in': _L3_gnn_in['W_in'], 'L3_gnn_W_out': _L3_gnn_in['W_out']}

def reference(x, adj, L0_gnn_t, L0_gnn_alpha, L0_gnn_W, L0_gnn_b, L1_gnn_W_self, L1_gnn_W_neigh, L2_gnn_v_node_feats, L2_gnn_uv_W1, L2_gnn_uv_b1, L2_gnn_uv_W2, L2_gnn_uv_b2, L2_gnn_uv_W3, L2_gnn_uv_b3, L2_gnn_vu_W1, L2_gnn_vu_b1, L2_gnn_vu_W2, L2_gnn_vu_b2, L2_gnn_vu_W3, L2_gnn_vu_b3, L3_gnn_W_in, L3_gnn_W_out):
    import jax
    import jax.numpy as jnp

    def _L0_gnn_ref(t, x, A, alpha, W, b):
        import jax, jax.numpy as jnp
        import numpy as np
        N = 4096
        H = 128
        a = alpha[0]
        A_prime = a * A
        diag = jnp.diagonal(A_prime) + (1.0 - a)
        A_prime = A_prime.at[jnp.arange(N), jnp.arange(N)].set(diag)
        out_degree = A_prime.sum(axis=1)
        inv_deg = jnp.where(out_degree == 0.0, 0.0, 1.0 / out_degree)
        x = inv_deg[:, None] * A_prime @ x
        x = x @ W.T + b
        return jax.nn.relu(x)

    def _L1_gnn_ref(h, adj, W_self, W_neigh):
        import jax, jax.numpy as jnp
        import numpy as np
        deg = jnp.clip(jnp.sum(adj, axis=1, keepdims=True), 1.0)
        h_neigh = adj @ h / deg
        return h @ W_self + h_neigh @ W_neigh

    def _L2_gnn_ref(u_node_feats, v_node_feats, uv_adj_mat, vu_adj_mat, uv_W1, uv_b1, uv_W2, uv_b2, uv_W3, uv_b3, vu_W1, vu_b1, vu_W2, vu_b2, vu_W3, vu_b3):
        import jax, jax.numpy as jnp
        import numpy as np
        NEG_SLOPE = 0.01
        N_U, N_V = (4096, 4096)
        U_F, V_F = (128, 128)
        HIDS = [128, 128]
        NUM_ROUNDS = 3

        def _glorot(key, fan_in, fan_out):
            lim = np.sqrt(6.0 / (fan_in + fan_out)).astype(np.float32)
            return jax.random.uniform(key, (fan_in, fan_out), jnp.float32, -lim, lim)

        def _mlp(x, W1, b1, W2, b2, W3, b3):
            a = jax.nn.leaky_relu
            x = a(x @ W1 + b1, NEG_SLOPE)
            x = a(x @ W2 + b2, NEG_SLOPE)
            return a(x @ W3 + b3, NEG_SLOPE)
        u, v = (u_node_feats, v_node_feats)
        for _ in range(NUM_ROUNDS):
            v = _mlp(uv_adj_mat @ u, uv_W1, uv_b1, uv_W2, uv_b2, uv_W3, uv_b3)
            u = _mlp(vu_adj_mat @ v, vu_W1, vu_b1, vu_W2, vu_b2, vu_W3, vu_b3)
        return v

    def _L3_gnn_ref(X, A, W_in, W_out):
        import jax, jax.numpy as jnp
        import numpy as np
        N = 8192
        IN_DIM = 128
        OUT_DIM = 128

        def _message(X, A, W):
            deg = jnp.sum(A, axis=1, keepdims=True)
            A_norm = A / jnp.where(deg > 0, deg, 1.0)
            return A_norm @ X @ W
        X_in = _message(X, A, W_in)
        X_out = _message(X, A.T, W_out)
        return X_in + X_out
    x = _layernorm(x + _L0_gnn_ref(L0_gnn_t, x, adj, L0_gnn_alpha, L0_gnn_W, L0_gnn_b), axis=-1)
    x = _layernorm(x + _L1_gnn_ref(x, adj, L1_gnn_W_self, L1_gnn_W_neigh), axis=-1)
    x = _layernorm(x + _L2_gnn_ref(x, L2_gnn_v_node_feats, adj, adj, L2_gnn_uv_W1, L2_gnn_uv_b1, L2_gnn_uv_W2, L2_gnn_uv_b2, L2_gnn_uv_W3, L2_gnn_uv_b3, L2_gnn_vu_W1, L2_gnn_vu_b1, L2_gnn_vu_W2, L2_gnn_vu_b2, L2_gnn_vu_W3, L2_gnn_vu_b3), axis=-1)
    x = _layernorm(x + _L3_gnn_ref(x, adj, L3_gnn_W_in, L3_gnn_W_out), axis=-1)
    return x

_drawn_inputs = setup_inputs


def setup_inputs(seed=0):
    import zlib

    import numpy as np

    out = dict(_drawn_inputs(seed))
    spreads = {'L0_gnn_b': (0.0, 0.1),
     'L2_gnn_uv_b1': (0.0, 0.282),
     'L2_gnn_uv_b2': (0.0, 0.1),
     'L2_gnn_uv_b3': (0.0, 0.1),
     'L2_gnn_vu_b1': (0.0, 0.334),
     'L2_gnn_vu_b2': (0.0, 0.1),
     'L2_gnn_vu_b3': (0.0, 0.1)}
    factors = {}
    for name, (base, spread) in spreads.items():
        noise = np.random.default_rng([zlib.crc32(name.encode()), seed]).standard_normal(out[name].shape)
        drawn = base * np.exp(spread * noise) if base else spread * noise
        out[name] = jnp.asarray(drawn.astype(out[name].dtype))
    for name, factor in factors.items():
        out[name] = (out[name] * factor).astype(out[name].dtype)
    return out
```

```python
from contextlib import ExitStack

import concourse.bass as bass
from concourse import mybir

F32 = mybir.dt.float32
F32R = mybir.dt.float32r
BF16 = mybir.dt.bfloat16
ALU = mybir.AluOpType
ACT = mybir.ActivationFunctionType
AX = mybir.AxisListType

P = 128
N = 4096
CH = 512
NCH = N // CH
QT = CH // P
JT = N // P
GJ = 4
NG = JT // GJ
GW = GJ * CH
RING = 4
HALF = 4
EPS = 1e-5
SLOPE = 0.01
NPROD = 9

DIFF, MEAN, MLP, MLP_NORM, INMSG, OUTMSG = range(6)
KIND = [DIFF, MEAN, MLP, MLP, MLP, MLP, MLP_NORM, INMSG, OUTMSG]
STEPS = {
    DIFF:     dict(turn=1, rows=3,                agg=2, std=6, hi=7,                       sums=5, stats=5, norm=6, lo=7),
    MEAN:     dict(turn=1, rows=2,                agg=3, std=6, hi=7,                       sums=5, stats=5, norm=6, lo=7),
    MLP:      dict(hid1=1, hid2=2, rows=3,        agg=3, lin1=4, lin2=5, hi=7,              act1=4, act2=5, sums=6, lo=7),
    MLP_NORM: dict(hid1=1, hid2=2, rows=3,        agg=3, lin1=4, lin2=5, std=7, hi=7,       act1=4, act2=5, sums=6, stats=6, norm=7, lo=7),
    INMSG:    dict(rows=1,                        agg=3,                                    sums=4),
    OUTMSG:   dict(rows=1,                        agg=3, std=5, hi=6,                       sums=4, stats=4, norm=5, lo=6),
}
NORMED = {0: 0, 1: 1, 6: 2, 8: 3}


def adj_resnorm(nc, x, at_blocks, a_blocks, mats, rows, cols, alpha, ident_d, out):
    with ExitStack() as ctx:
        def sb(name, shape, dt=F32):
            return ctx.enter_context(nc.sbuf_tensor(name, shape, dt))

        def psum(name, shape):
            return ctx.enter_context(nc.psum_tensor(name, shape, F32))

        def sem(name):
            return ctx.enter_context(nc.semaphore(name))

        raw = sb("raw", [P, RING, GW])
        a_hi = sb("a_hi", [P, HALF, GW], F32R)
        a_lo = sb("a_lo", [P, HALF, GW], F32R)
        x_res = sb("x_res", [P, JT * P])
        x_hi, x_hi_at, x_lo, x_lo_at = [], [], [], []
        for i in range(2):
            for name, halves, at in (("x_hi", x_hi, x_hi_at), ("x_lo", x_lo, x_lo_at)):
                halves.append(sb(f"{name}{i}", [P, JT * P], F32R))
                at.append(nc.sbuf_base - 4 * JT * P)
        x_in = nc.alloc_sbuf_tensor_at("x_in", [P, JT * P], F32, offset=x_hi_at[1])
        acc = nc.alloc_sbuf_tensor_at("acc", [P, GW], F32, offset=x_lo_at[1])
        junk = nc.alloc_sbuf_tensor_at("junk", [P, GJ, CH], BF16, offset=x_lo_at[1] + 4 * GW)
        agg = sb("agg", [P, CH])
        hid1 = sb("hid1", [P, CH])
        hid2 = sb("hid2", [P, CH])
        lin1, lin2 = sb("lin1", [P, CH]), sb("lin2", [P, CH])
        rows_in = sb("rows_in", [P, CH])
        biased = sb("biased", [P, CH])
        pre = sb("pre", [P, CH])
        rows_out = sb("rows_out", [P, CH])
        fold = sb("fold", [P, CH])
        col_part = sb("col_part", [P, NCH * JT])
        stats = sb("stats", [P, QT, 6])
        mean2, gap, squares, mean, gap2, var = (sb(k, [P, QT]) for k in ("mean2", "gap", "squares", "mean", "gap2", "var"))
        std = sb("std", [P, QT])
        rstd = sb("rstd", [P, QT])
        deg_mix = sb("deg_mix", [P, QT])
        deg_safe = sb("deg_safe", [P, QT])
        deg_some = sb("deg_some", [P, QT])
        deg_rec = sb("deg_rec", [P, QT])
        inv_diff = sb("inv_diff", [P, QT])
        row_sum = sb("row_sum", [P, JT])
        deg = sb("deg", [P, 3, JT])
        positive = sb("positive", [P, 2, JT])
        other = sb("other", [P, 2, JT])
        inv_deg = sb("inv_deg", [P, 3, JT])
        eps_t = sb("eps_t", [P, 1])
        ones = sb("ones", [P, 1])
        alpha_t = sb("alpha_t", [P, 1])
        one_less = sb("one_less", [P, 1])
        ident = sb("ident", [P, P])
        w = {name: sb("w_" + name, [P, P]) for name in mats}
        row_bias = {name: sb("rb_" + name, [P, P]) for name in rows}
        col_bias = {name: sb("cb_" + name, [P, 1]) for name in cols}

        ps_main = [psum(f"ps_main{i}", [P, CH]) for i in range(2)]
        ps_hid1 = psum("ps_hid1", [P, CH])
        ps_hid2 = psum("ps_hid2", [P, CH])
        ps_rows = psum("ps_rows", [P, CH])
        ps_deg = psum("ps_deg", [P, QT])

        consts_in = sem("consts_in")
        raw_in = [sem(f"raw_in{i}") for i in range(RING)]
        act_groups = sem("act_groups")
        dve_groups = sem("dve_groups")
        pe_groups = sem("pe_groups")
        set_up = sem("set_up")
        agg_copied = sem("agg_copied")
        rows_taken = sem("rows_taken")
        turned = sem("turned")
        turn_copied = sem("turn_copied")
        hid1_done = sem("hid1_done")
        lin1_done = sem("lin1_done")
        hid1_copied = sem("hid1_copied")
        hid2_done = sem("hid2_done")
        lin2_done = sem("lin2_done")
        hid2_copied = sem("hid2_copied")
        rows_done = sem("rows_done")
        rows_read = sem("rows_read")
        folded = sem("folded")
        deg_step = sem("deg_step")
        lrelu_done = sem("lrelu_done")
        mlp_hi_done = sem("mlp_hi_done")
        pre_done = sem("pre_done")
        stats_done = sem("stats_done")
        moment_step = sem("moment_step")
        moments_done = sem("moments_done")
        std_done = sem("std_done")
        rstd_done = sem("rstd_done")
        norm_done = sem("norm_done")
        x_hi_done = sem("x_hi_done")
        x_done = sem("x_done")
        prep = sem("prep")
        stored = sem("stored")

        def source(p):
            return [None, 0, 1, 0, 1, 0, 1, 0, 0][p]

        def target(p):
            return [0, 1, 0, 1, 0, 1, 0][p]

        def norm_index(p, e):
            return e - NCH * p + NCH * NORMED[p]

        def chunk(t, c):
            h, b = c
            return t[:, :].rearrange("p (h b n) -> p h b n", b=2, n=CH)[:, h, b, :]

        def per_row(t, c, q):
            h, b = c
            return t.rearrange("p (h b q) -> p h b q", b=2, q=QT)[:, h, b, q:q + 1]

        def previous(p, h, b):
            if b:
                return p, (h, 0)
            if isinstance(h, int) and h == 0:
                return p - 1, (NCH // 2 - 1, 1)
            return p, (h - 1, 1)

        def tile(t, q):
            return t[:, q * P:(q + 1) * P]

        def chunks(eng, slot, p):
            slot(p, 0, 0)
            slot(p, 0, 1)
            with eng.Fori(1, NCH // 2) as h:
                slot(p, h, 0)
                slot(p, h, 1)

        block = ctx.enter_context(nc.Block())

        @block.sync
        def _(sp):
            small = [(w[k], mats[k]) for k in mats] + [(ident, ident_d)]
            small += [(col_bias[k], cols[k].rearrange("(p a) -> p a", a=1)) for k in cols]
            small += [(row_bias[k], rows[k].rearrange("(a f) -> a f", a=1).to_broadcast([P, P])) for k in rows]
            small += [(alpha_t, alpha.rearrange("(a f) -> a f", a=1).to_broadcast([P, 1]))]

            def slot(p, h, b):
                s = NCH * p + 2 * h + b
                src = a_blocks if p == NPROD - 1 else at_blocks
                src = src.rearrange("(h b) g p n -> h b g p n", b=2)
                for g in range(NG):
                    t = NG * s + g
                    if not (isinstance(t, int) and t < RING):
                        sp.wait_ge(dve_groups, t - RING + 1)
                        if p == 0 or (p == 1 and isinstance(h, int) and h == 0 and b == 0 and g < RING):
                            sp.wait_ge(act_groups, t - RING + 1)
                            sp.wait_ge(pe_groups, t - RING + 1)
                    sp.dma_start(raw[:, g % RING, :], src[h, b, g]).then_inc(raw_in[g % RING], 16)
                    if isinstance(t, int) and t == 0:
                        sp.dma_start(x_in[:, :], x).then_inc(consts_in, 16)
                        for dst, s_ in small:
                            sp.dma_start(dst[:, :], s_).then_inc(consts_in, 16)

            for p in range(NPROD):
                chunks(sp, slot, p)

        n_const = 16 * (2 + len(mats) + len(cols) + len(rows) + 1)

        @block.scalar
        def _(act):
            def group(p, h, b, g):
                s = NCH * p + 2 * h + b
                t = NG * s + g
                act.wait_ge(raw_in[g % RING], 16 * (2 * s + g // RING + 1))
                if p == 0:
                    if not (isinstance(t, int) and t == 0):
                        act.wait_ge(act_groups, t)
                    for j in range(GJ):
                        part = col_part[:, :].rearrange("p (h b j) -> p h b j", b=2, j=JT)
                        last = nc.scalar.activation(junk[:, j, :], raw[:, g % RING, j * CH:(j + 1) * CH], ACT.Copy,
                                                    accum_out=part[:, h, b, GJ * g + j:GJ * g + j + 1])
                    last.then_inc(act_groups, 1)
                else:
                    if not (p == 1 and isinstance(h, int) and h == 0 and b == 0 and g < HALF):
                        act.wait_ge(pe_groups, t - HALF + 1)
                    nc.scalar.copy(a_hi[:, g % HALF, :], raw[:, g % RING, :]).then_inc(act_groups, 1)

            def epilogue(p, c, g):
                kind, e = KIND[p], NCH * p + 2 * c[0] + c[1]
                at = STEPS[kind]
                n = e - NCH * 2
                if g == 0 and kind in (DIFF, MEAN):
                    if not (isinstance(e, int) and e == 0):
                        act.wait_ge(turned, e)
                    nc.scalar.copy(rows_in[:, :], chunk(x_in if kind == DIFF else x_res, c)).then_inc(rows_taken, 1)
                if g == at["agg"]:
                    act.wait_ge(pe_groups, NG * (e + 1))
                    if not (isinstance(e, int) and e == 0):
                        act.wait_ge(rows_done, e)
                    if kind == DIFF:
                        nc.scalar.activation(agg[:, :], ps_main[c[1]][:, :], ACT.Copy,
                                             scale=alpha_t[:, :]).then_inc(agg_copied, 1)
                    else:
                        nc.scalar.copy(agg[:, :], ps_main[c[1]][:, :]).then_inc(agg_copied, 1)
                    if kind in (DIFF, MEAN):
                        act.wait_ge(turned, e + 1)
                        if kind == DIFF:
                            act.wait_ge(set_up, 1)
                            nc.scalar.activation(hid1[:, :], ps_hid1[:, :], ACT.Copy,
                                                 scale=one_less[:, :]).then_inc(turn_copied, 1)
                        else:
                            nc.scalar.copy(hid1[:, :], ps_hid1[:, :]).then_inc(turn_copied, 1)
                if g == at.get("lin1"):
                    bias = col_bias["uv_b1" if p % 2 == 0 else "vu_b1"]
                    act.wait_ge(hid1_done, n + 1)
                    nc.scalar.activation(lin1[:, :], ps_hid1[:, :], ACT.Identity, bias=bias[:, :]).then_inc(lin1_done, 1)
                if g == at.get("lin2"):
                    bias = col_bias["uv_b2" if p % 2 == 0 else "vu_b2"]
                    act.wait_ge(hid2_done, n + 1)
                    nc.scalar.activation(lin2[:, :], ps_hid2[:, :], ACT.Identity, bias=bias[:, :]).then_inc(lin2_done, 1)
                if g == at.get("hi") and kind == MLP:
                    act.wait_ge(lrelu_done, n + 1)
                    nc.scalar.copy(chunk(x_hi[target(p)], c), rows_out[:, :]).then_inc(mlp_hi_done, 1)
                if p in NORMED:
                    k = norm_index(p, e)
                    if g == at["std"]:
                        act.wait_ge(moments_done, k + 1)
                        nc.scalar.activation(std[:, :], var[:, :], ACT.Sqrt, bias=eps_t[:, :]).then_inc(std_done, 1)
                    if g == at["hi"] and kind != OUTMSG:
                        act.wait_ge(norm_done, k + 1)
                        nc.scalar.copy(chunk(x_hi[target(p)], c), rows_out[:, :])
                        nc.scalar.copy(chunk(x_res, c), rows_out[:, :]).then_inc(x_hi_done, 1)
                    if g == at["hi"] and kind == OUTMSG:
                        act.wait_ge(norm_done, k + 1)
                        dst = out.rearrange("(h b q p) f -> h b p q f", b=2, q=QT, p=P)[c[0], c[1]]
                        act.dma_start(dst, rows_out[:, :].rearrange("p (q f) -> p q f", q=QT)).then_inc(stored, 16)

            def slot(p, h, b):
                for g in range(NG):
                    if not (p == 0 and isinstance(h, int) and h == 0 and b == 0):
                        epilogue(*previous(p, h, b), g)
                    group(p, h, b, g)

            act.wait_ge(consts_in, n_const)
            for p in range(NPROD):
                chunks(act, slot, p)
            for g in range(NG):
                epilogue(NPROD - 1, (NCH // 2 - 1, 1), g)
            act.wait_ge(stored, 16 * NCH)

        @block.vector
        def _(dve):
            def group(p, h, b, g):
                s = NCH * p + 2 * h + b
                t = NG * s + g
                first = isinstance(t, int) and t == 0
                if p == 0:
                    dve.wait_ge(raw_in[g % RING], 16 * (2 * s + g // RING + 1))
                    if g == 0:
                        if not first:
                            dve.wait_ge(folded, s)
                        nc.vector.tensor_copy(acc[:, :], raw[:, g % RING, :]).then_inc(dve_groups, 1)
                    else:
                        dve.wait_ge(dve_groups, t)
                        nc.vector.tensor_tensor(acc[:, :], acc[:, :], raw[:, g % RING, :],
                                                ALU.add).then_inc(dve_groups, 1)
                    if g == NG - 1:
                        dve.wait_ge(dve_groups, t + 1)
                        nc.vector.tensor_reduce(fold[:, :], acc[:, :].rearrange("p (j n) -> p n j", j=GJ),
                                                AX.X, ALU.add).then_inc(folded, 1)
                else:
                    if not (p == 1 and isinstance(h, int) and h == 0 and b == 0 and g < HALF):
                        dve.wait_ge(pe_groups, t - HALF + 1)
                    dve.wait_ge(act_groups, t + 1)
                    nc.vector.tensor_tensor(a_lo[:, g % HALF, :], raw[:, g % RING, :],
                                            a_hi[:, g % HALF, :].bitcast(F32), ALU.subtract).then_inc(dve_groups, 1)

            def epilogue(p, c, g):
                kind, e = KIND[p], NCH * p + 2 * c[0] + c[1]
                at = STEPS[kind]
                normed = p in NORMED
                k = norm_index(p, e) if normed else None
                n = e - NCH * 2
                for step, lin, lin_done, hid, done in (("act1", lin1, lin1_done, hid1, hid1_copied),
                                                       ("act2", lin2, lin2_done, hid2, hid2_copied)):
                    if g == at.get(step):
                        dve.wait_ge(lin_done, n + 1)
                        nc.vector.scalar_tensor_tensor(hid[:, :], lin[:, :], SLOPE, lin[:, :],
                                                       ALU.mult, ALU.max).then_inc(done, 1)
                if g == at["sums"]:
                    dve.wait_ge(rows_done, e + 1)
                    if kind == DIFF:
                        nc.vector.tensor_copy(per_row4(row_sum[:, :], c), ps_deg[:, :])
                        nc.vector.tensor_scalar(deg_mix[:, :], ps_deg[:, :], alpha_t[:, :], one_less[:, :],
                                                ALU.mult, ALU.add).then_inc(deg_step, 1)
                        dve.wait_ge(deg_step, 4 * e + 1)
                        nc.vector.scalar_tensor_tensor(deg_safe[:, :], deg_mix[:, :], 0.0, deg_mix[:, :],
                                                       ALU.is_equal, ALU.add)
                        nc.vector.tensor_scalar(deg_some[:, :], deg_mix[:, :], 0.0, None,
                                                ALU.not_equal).then_inc(deg_step, 1)
                        dve.wait_ge(deg_step, 4 * e + 2)
                        nc.vector.reciprocal(deg_rec[:, :], deg_safe[:, :]).then_inc(deg_step, 1)
                        dve.wait_ge(deg_step, 4 * e + 3)
                        nc.vector.tensor_tensor(inv_diff[:, :], deg_rec[:, :], deg_some[:, :],
                                                ALU.mult).then_inc(deg_step, 1)
                        dve.wait_ge(deg_step, 4 * e + 4)
                        for q in range(QT):
                            last = nc.vector.scalar_tensor_tensor(tile(biased, q), tile(ps_rows, q), inv_diff[:, q:q + 1],
                                                                  row_bias["b"][:, :], ALU.mult, ALU.add)
                        last.then_inc(rows_read, 1)
                        dve.wait_ge(rows_read, e + 1)
                        nc.vector.scalar_tensor_tensor(pre[:, :], biased[:, :], 0.0, chunk(x_in, c),
                                                       ALU.max, ALU.add).then_inc(pre_done, 1)
                    elif kind == MEAN:
                        for q in range(QT):
                            last = nc.vector.scalar_tensor_tensor(tile(biased, q), tile(ps_rows, q), per_row(inv_deg[:, 0, :], c, q),
                                                                  chunk_tile(x_res, c, q), ALU.mult, ALU.add)
                        last.then_inc(rows_read, 1)
                        dve.wait_ge(rows_read, e + 1)
                        nc.vector.tensor_tensor(pre[:, :], biased[:, :], ps_hid2[:, :], ALU.add).then_inc(pre_done, 1)
                    elif kind in (MLP, MLP_NORM):
                        b3 = row_bias["uv_b3" if p % 2 == 0 else "vu_b3"]
                        nc.vector.tensor_tensor(biased[:, :].rearrange("p (q f) -> p q f", q=QT),
                                                ps_rows[:, :].rearrange("p (q f) -> p q f", q=QT),
                                                b3[:, :].rearrange("p (a f) -> p a f", a=1).to_broadcast([P, QT, P]),
                                                ALU.add).then_inc(rows_read, 1)
                        dve.wait_ge(rows_read, e + 1)
                        nc.vector.scalar_tensor_tensor(rows_out[:, :], biased[:, :], SLOPE, biased[:, :],
                                                       ALU.mult, ALU.max).then_inc(lrelu_done, 1)
                    elif kind == INMSG:
                        for q in range(QT):
                            r = chunk_tile(x_res, c, q)
                            last = nc.vector.scalar_tensor_tensor(r, tile(ps_rows, q), per_row(inv_deg[:, 1, :], c, q),
                                                                  r, ALU.mult, ALU.add)
                        last.then_inc(rows_read, 1)
                    else:
                        for q in range(QT):
                            last = nc.vector.scalar_tensor_tensor(tile(pre, q), tile(ps_rows, q), per_row(inv_deg[:, 2, :], c, q),
                                                                  chunk_tile(x_res, c, q), ALU.mult, ALU.add)
                        last.then_inc(rows_read, 1)
                if kind == MLP and g == at["lo"]:
                    dve.wait_ge(mlp_hi_done, e - 2 * NCH + 1)
                    nc.vector.tensor_tensor(chunk(x_lo[target(p)], c), rows_out[:, :],
                                            chunk(x_hi[target(p)], c).bitcast(F32), ALU.subtract).then_inc(x_done, 1)
                if kind == MLP_NORM and g == at["stats"]:
                    dve.wait_ge(lrelu_done, e - 2 * NCH + 1)
                    nc.vector.tensor_tensor(pre[:, :], rows_out[:, :], chunk(x_res, c), ALU.add).then_inc(pre_done, 1)
                if not normed:
                    return
                if g == at["stats"]:
                    if kind == OUTMSG:
                        dve.wait_ge(rows_read, e + 1)
                    else:
                        dve.wait_ge(pre_done, k + 1)
                    for q in range(QT):
                        last = nc.vector.bn_stats(stats[:, q, :], tile(pre, q))
                    last.then_inc(stats_done, 1)
                    dve.wait_ge(stats_done, k + 1)
                    nc.vector.tensor_tensor(mean2[:, :], stats[:, :, 1], stats[:, :, 4], ALU.add)
                    nc.vector.tensor_tensor(gap[:, :], stats[:, :, 1], stats[:, :, 4], ALU.subtract)
                    nc.vector.tensor_tensor(squares[:, :], stats[:, :, 2], stats[:, :, 5],
                                            ALU.add).then_inc(moment_step, 1)
                    dve.wait_ge(moment_step, 2 * k + 1)
                    nc.vector.tensor_scalar(mean[:, :], mean2[:, :], 0.5, None, ALU.mult)
                    nc.vector.scalar_tensor_tensor(gap2[:, :], gap[:, :], 0.25, gap[:, :],
                                                   ALU.mult, ALU.mult).then_inc(moment_step, 1)
                    dve.wait_ge(moment_step, 2 * k + 2)
                    nc.vector.scalar_tensor_tensor(var[:, :], squares[:, :], 1.0 / P, gap2[:, :],
                                                   ALU.mult, ALU.add).then_inc(moments_done, 1)
                if g == at["norm"]:
                    dve.wait_ge(std_done, k + 1)
                    nc.vector.reciprocal(rstd[:, :], std[:, :]).then_inc(rstd_done, 1)
                    dve.wait_ge(rstd_done, k + 1)
                    if kind == OUTMSG and not (isinstance(e, int) and e == NCH * p):
                        dve.wait_ge(stored, 16 * (e - NCH * p))
                    for q in range(QT):
                        last = nc.vector.tensor_scalar(tile(rows_out, q), tile(pre, q), mean[:, q:q + 1], rstd[:, q:q + 1],
                                                       ALU.subtract, ALU.mult)
                    last.then_inc(norm_done, 1)
                if g == at["lo"] and kind != OUTMSG:
                    dve.wait_ge(x_hi_done, k + 1)
                    nc.vector.tensor_tensor(chunk(x_lo[target(p)], c), rows_out[:, :],
                                            chunk(x_hi[target(p)], c).bitcast(F32), ALU.subtract).then_inc(x_done, 1)

            def per_row4(t, c):
                return t.rearrange("p (h b q) -> p h b q", b=2, q=QT)[:, c[0], c[1], :]

            def chunk_tile(t, c, q):
                return t[:, :].rearrange("p (h b q f) -> p h b q f", b=2, q=QT, f=P)[:, c[0], c[1], q, :]

            def degrees():
                dve.wait_ge(act_groups, NCH * NG)
                dve.wait_ge(rows_read, NCH)
                nc.vector.tensor_reduce(deg[:, 2, :], col_part[:, :].rearrange("p (c j) -> p j c", c=NCH), AX.X, ALU.add)
                nc.vector.tensor_copy(deg[:, 1, :], row_sum[:, :])
                nc.vector.tensor_scalar(deg[:, 0, :], row_sum[:, :], 1.0, None, ALU.max).then_inc(prep, 1)
                dve.wait_ge(prep, 1)
                nc.vector.tensor_scalar(positive[:, :, :], deg[:, 1:3, :], 0.0, None, ALU.is_gt)
                nc.vector.tensor_scalar(other[:, :, :], deg[:, 1:3, :], 0.0, None, ALU.is_le).then_inc(prep, 1)
                dve.wait_ge(prep, 2)
                nc.vector.tensor_tensor(deg[:, 1:3, :], deg[:, 1:3, :], positive[:, :, :], ALU.mult).then_inc(prep, 1)
                dve.wait_ge(prep, 3)
                nc.vector.tensor_tensor(deg[:, 1:3, :], deg[:, 1:3, :], other[:, :, :], ALU.add).then_inc(prep, 1)
                dve.wait_ge(prep, 4)
                nc.vector.reciprocal(inv_deg[:, :, :], deg[:, :, :]).then_inc(prep, 1)
                dve.wait_ge(prep, 5)

            def slot(p, h, b):
                for g in range(NG):
                    if not (p == 0 and isinstance(h, int) and h == 0 and b == 0):
                        epilogue(*previous(p, h, b), g)
                    group(p, h, b, g)
                if p == 1 and isinstance(h, int) and h == 0 and b == 0:
                    degrees()

            nc.vector.memset(eps_t[:, :], EPS)
            nc.vector.memset(ones[:, :], 1.0)
            dve.wait_ge(consts_in, n_const)
            nc.vector.tensor_scalar(one_less[:, :], alpha_t[:, :], -1.0, 1.0, ALU.mult, ALU.add).then_inc(set_up, 1)
            dve.wait_ge(set_up, 1)
            for p in range(NPROD):
                chunks(dve, slot, p)
            for g in range(NG):
                epilogue(NPROD - 1, (NCH // 2 - 1, 1), g)

        @block.tensor
        def _(pe):
            def group(p, h, b, g):
                s = NCH * p + 2 * h + b
                t = NG * s + g
                if g == 0 and not (isinstance(s, int) and s < 2):
                    pe.wait_ge(agg_copied, s - 1)
                if p == 0:
                    pe.wait_ge(raw_in[g % RING], 16 * (2 * s + g // RING + 1))
                    for j in range(GJ):
                        jt = GJ * g + j
                        last = nc.tensor.matmul(ps_main[b][:, :], tile(x_in, jt), raw[:, g % RING, j * CH:(j + 1) * CH],
                                                start=jt == 0, stop=jt == JT - 1)
                else:
                    if p < NPROD - 1 and isinstance(h, int) and h == 0 and b == 0:
                        pe.wait_ge(x_done, NCH * (p - 1) + g + 1)
                    pe.wait_ge(dve_groups, t + 1)
                    hi, lo = x_hi[source(p)], x_lo[source(p)]
                    for j in range(GJ):
                        jt = GJ * g + j
                        block_hi = a_hi[:, g % HALF, j * CH:(j + 1) * CH]
                        block_lo = a_lo[:, g % HALF, j * CH:(j + 1) * CH]
                        nc.tensor.matmul(ps_main[b][:, :], tile(hi, jt), block_hi, start=jt == 0, stop=False)
                        nc.tensor.matmul(ps_main[b][:, :], tile(hi, jt), block_lo, start=False, stop=False)
                        last = nc.tensor.matmul(ps_main[b][:, :], tile(lo, jt), block_hi, start=False, stop=jt == JT - 1)
                last.then_inc(pe_groups, 1)

            def by_rows(ps, lhs, weight, more=()):
                for q in range(QT):
                    last = nc.tensor.matmul(tile(ps, q), tile(lhs, q), weight[:, :], start=True, stop=not more)
                    for lhs2, weight2 in more:
                        last = nc.tensor.matmul(tile(ps, q), tile(lhs2, q), weight2[:, :], start=False, stop=True)
                return last

            def epilogue(p, c, g):
                kind, e = KIND[p], NCH * p + 2 * c[0] + c[1]
                at = STEPS[kind]
                n = e - NCH * 2
                tag = "uv" if p % 2 == 0 else "vu"
                if g == at.get("turn"):
                    pe.wait_ge(rows_taken, e + 1)
                    if not (isinstance(e, int) and e == 0):
                        pe.wait_ge(turn_copied, e)
                    for q in range(QT):
                        last = nc.tensor.transpose(tile(ps_hid1, q), tile(rows_in, q), ident[:, :])
                    last.then_inc(turned, 1)
                if g == at.get("hid1"):
                    pe.wait_ge(agg_copied, e + 1)
                    nc.tensor.matmul(ps_hid1[:, :], w[tag + "_W1"][:, :], agg[:, :], start=True, stop=True).then_inc(hid1_done, 1)
                if g == at.get("hid2"):
                    pe.wait_ge(hid1_copied, n + 1)
                    if p == 2 and isinstance(e, int) and e == NCH * p:
                        pe.wait_ge(pre_done, e)
                    nc.tensor.matmul(ps_hid2[:, :], w[tag + "_W2"][:, :], hid1[:, :], start=True, stop=True).then_inc(hid2_done, 1)
                if g == at["rows"]:
                    if not (isinstance(e, int) and e == 0):
                        pe.wait_ge(rows_read, e)
                    pe.wait_ge(agg_copied, e + 1)
                    if kind == DIFF:
                        pe.wait_ge(turn_copied, e + 1)
                        pe.wait_ge(folded, e + 1)
                        by_rows(ps_rows, agg, w["W_t"], [(hid1, w["W_t"])])
                        for q in range(QT):
                            last = nc.tensor.matmul(ps_deg[:, q:q + 1], tile(fold, q), ones[:, :], start=True, stop=True)
                    elif kind == MEAN:
                        pe.wait_ge(turn_copied, e + 1)
                        pe.wait_ge(pre_done, e)
                        by_rows(ps_rows, agg, w["W_neigh"])
                        last = by_rows(ps_hid2, hid1, w["W_self"])
                    elif kind in (MLP, MLP_NORM):
                        pe.wait_ge(hid2_copied, n + 1)
                        last = by_rows(ps_rows, hid2, w[tag + "_W3"])
                    else:
                        last = by_rows(ps_rows, agg, w["W_in" if kind == INMSG else "W_out"])
                    last.then_inc(rows_done, 1)

            def slot(p, h, b):
                for g in range(NG):
                    if not (p == 0 and isinstance(h, int) and h == 0 and b == 0):
                        epilogue(*previous(p, h, b), g)
                    group(p, h, b, g)

            pe.wait_ge(consts_in, n_const)
            for p in range(NPROD):
                chunks(pe, slot, p)
            for g in range(NG):
                epilogue(NPROD - 1, (NCH // 2 - 1, 1), g)


MATS = {"W_t": ("L0_gnn_W", True), "W_self": ("L1_gnn_W_self", False), "W_neigh": ("L1_gnn_W_neigh", False),
        "W_in": ("L3_gnn_W_in", False), "W_out": ("L3_gnn_W_out", False)}
MATS |= {f"{t}_W{i}": (f"L2_gnn_{t}_W{i}", False) for t in ("uv", "vu") for i in (1, 2, 3)}
ROWS = {"b": "L0_gnn_b", "uv_b3": "L2_gnn_uv_b3", "vu_b3": "L2_gnn_vu_b3"}
COLS = {f"{t}_b{i}": f"L2_gnn_{t}_b{i}" for t in ("uv", "vu") for i in (1, 2)}


def blocks(a, np):
    a = a.reshape(NG, GJ, P, NCH, CH).transpose(3, 0, 2, 1, 4)
    return np.ascontiguousarray(a).reshape(NCH, NG, P, GW)


def kernel(**inputs):
    import numpy as np
    import concourse.bacc as bacc
    from concourse.bass_utils import run_bass_kernel_spmd as run

    nc = bacc.Bacc("TRN2", target_bir_lowering=False, num_devices=1, dynamic_dma_scratch_size=512)
    arrays = {}

    def give(name, a):
        name = "in_" + name
        arrays[name] = np.ascontiguousarray(a)
        return nc.dram_tensor(name, arrays[name].shape, mybir.dt.from_np(arrays[name].dtype), kind="ExternalInput").ap()

    adj = np.asarray(inputs["adj"])
    x = np.asarray(inputs["x"])
    x_d = give("x", x.reshape(JT, P, P).transpose(1, 0, 2).reshape(P, JT * P))
    at_d = give("at", blocks(adj.T, np))
    a_d = give("a", blocks(adj, np))
    mats = {k: give(k, np.asarray(inputs[s]).T if t else np.asarray(inputs[s])) for k, (s, t) in MATS.items()}
    rows = {k: give(k, np.asarray(inputs[s])) for k, s in ROWS.items()}
    cols = {k: give(k, np.asarray(inputs[s])) for k, s in COLS.items()}
    alpha = give("alpha", np.asarray(inputs["L0_gnn_alpha"]))
    ident = give("ident", np.eye(P, dtype=np.float32))
    out = nc.dram_tensor("out", (N, P), F32, kind="ExternalOutput").ap()
    adj_resnorm(nc, x_d, at_d, a_d, mats, rows, cols, alpha, ident, out)
    r = run(nc, [arrays], core_ids=[0])
    return r.results[0]["out"]
```

```python
from collections import namedtuple
from contextlib import ExitStack

import concourse.bass as bass
from concourse import mybir

F32 = mybir.dt.float32
F32R = mybir.dt.float32r
BF16 = mybir.dt.bfloat16
ALU = mybir.AluOpType
ACT = mybir.ActivationFunctionType
AX = mybir.AxisListType

P = 128
N = 4096
CH = 512
NCH = N // CH
QT = CH // P
JT = N // P
GJ = 4
NG = JT // GJ
GW = GJ * CH
RING = 4
HALF = 4
EPS = 1e-5
SLOPE = 0.01
NPROD = 9

DIFF, MEAN, MLP, MLP_NORM, INMSG, OUTMSG = range(6)
KIND = [DIFF, MEAN, MLP, MLP, MLP, MLP, MLP_NORM, INMSG, OUTMSG]
STEPS = {
    DIFF:     dict(turn=1, rows=3,          agg=2, std=6, hi=7,                 mix=3, sums=5, stats=5, norm=6, lo=7),
    MEAN:     dict(turn=1, rows=2,          agg=3, std=6, hi=7,                 sums=5, stats=5, norm=6, lo=7),
    MLP:      dict(hid1=1, hid2=2, rows=3,  agg=3, lin1=4, lin2=5, hi=7,        act1=4, act2=5, sums=6, lo=7),
    MLP_NORM: dict(hid1=1, hid2=2, rows=3,  agg=3, lin1=4, lin2=5, std=7, hi=8, act1=4, act2=5, sums=6, stats=6, norm=7, lo=8),
    INMSG:    dict(rows=2,                  agg=3,                              sums=4),
    OUTMSG:   dict(rows=2,                  agg=3, std=6, hi=7,                 sums=5, stats=5, norm=6),
}
LATEST = 10

LEADS = {2: 0, 4: 1, 6: 2}
FOLLOWS = {3: 0, 5: 1, 7: 2}
FOLLOWER_ORDER = [0, 7, 1, 6, 2, 5, 3, 4]


def order_of(p):
    return FOLLOWER_ORDER if p in FOLLOWS else list(range(NCH))


def groups_of(p, i):
    if p in FOLLOWS:
        return list(range(i, NG))
    if p and i == 0:
        return order_of(p - 1)
    if p in LEADS:
        return [g for g in range(NG) if g != i - 1] + [i - 1]
    return list(range(NG))


LOADS = [sum(len(groups_of(p, i)) for i in range(NCH)) for p in range(NPROD)]
FIRST_LOAD = [sum(LOADS[:p]) for p in range(NPROD + 1)]

Slot = namedtuple("Slot", "p c e groups t0")


def slot_at(p, k, b=None):
    if b is not None and not isinstance(k, int):
        return Slot(p, (k, b), NCH * p + 2 * k + b, list(range(NG)), FIRST_LOAD[p] + NG * b + 2 * NG * k)
    k = k if b is None else 2 * k + b
    order = order_of(p)
    t0 = FIRST_LOAD[p] + sum(len(groups_of(p, i)) for i in order[:k])
    return Slot(p, divmod(order[k], 2), NCH * p + k, groups_of(p, order[k]), t0)


def chunks(eng, p):
    def fixed(k):
        slot = slot_at(p, k)
        before = [slot_at(*divmod(e, NCH)) for e in range(max(0, slot.e - LATEST - 1), slot.e)]
        return slot, [[(s, slot.t0 + n - s.t0 - len(s.groups)) for s in before
                       if slot.t0 + n - s.t0 - len(s.groups) <= LATEST] for n in range(len(slot.groups))]

    if p in LEADS or p in FOLLOWS:
        for k in range(NCH):
            yield fixed(k)
    else:
        yield fixed(0)
        yield fixed(1)
        with eng.Fori(1, NCH // 2) as h:
            for b in range(2):
                last, last_but_one = slot_before(p, h, b, 1), slot_before(p, h, b, 2)
                yield slot_at(p, h, b), [[(last_but_one, n + NG)] * (n + NG <= LATEST) + [(last, n)]
                                         for n in range(NG)]


def slot_before(p, h, b, back):
    i = b - back
    return Slot(p, (h + i // 2, i % 2), NCH * p + i + 2 * h, list(range(NG)), FIRST_LOAD[p] + NG * i + 2 * NG * h)


def last_steps():
    last = slot_at(NPROD - 1, NCH - 1)
    return [(last, n) for n in range(LATEST + 1)]


def number(slot):
    return 2 * slot.c[0] + slot.c[1]


def is_first(value, bound=1):
    return isinstance(value, int) and value < bound


NORMED = {0: 0, 1: 1, 6: 2, 8: 3}


def adj_resnorm(nc, x, at_blocks, a_blocks, mats, rows, cols, alpha, ident_d, out):
    with ExitStack() as ctx:
        def sb(name, shape, dt=F32):
            return ctx.enter_context(nc.sbuf_tensor(name, shape, dt))

        def psum(name, shape):
            return ctx.enter_context(nc.psum_tensor(name, shape, F32))

        def sem(name):
            return ctx.enter_context(nc.semaphore(name))

        raw = sb("raw", [P, RING, GW])
        a_hi = sb("a_hi", [P, HALF, GW], F32R)
        a_lo = sb("a_lo", [P, HALF, GW], F32R)
        x_res = sb("x_res", [P, JT * P])
        x_hi, x_hi_at, x_lo, x_lo_at = [], [], [], []
        for i in range(2):
            for name, halves, at in (("x_hi", x_hi, x_hi_at), ("x_lo", x_lo, x_lo_at)):
                halves.append(sb(f"{name}{i}", [P, JT * P], F32R))
                at.append(nc.sbuf_base - 4 * JT * P)
        x_in = nc.alloc_sbuf_tensor_at("x_in", [P, JT * P], F32, offset=x_hi_at[1])
        acc = nc.alloc_sbuf_tensor_at("acc", [P, GW], F32, offset=x_lo_at[1])
        junk = nc.alloc_sbuf_tensor_at("junk", [P, GJ, CH], BF16, offset=x_lo_at[1] + 4 * GW)
        agg = sb("agg", [P, CH])
        hid1 = sb("hid1", [P, CH])
        hid2 = sb("hid2", [P, CH])
        lin1, lin2 = sb("lin1", [P, CH]), sb("lin2", [P, CH])
        rows_in = lin1
        lrelu3 = sb("lrelu3", [P, CH])
        partial = sb("partial", [P, NCH - 1, CH])
        biased = sb("biased", [P, CH])
        pre = sb("pre", [P, CH])
        rows_out = sb("rows_out", [P, CH])
        fold = sb("fold", [P, CH])
        col_part = sb("col_part", [P, NCH * JT])
        stats = sb("stats", [P, QT, 6])
        mean2, gap, squares, mean, gap2, var = (sb(k, [P, QT]) for k in ("mean2", "gap", "squares", "mean", "gap2", "var"))
        std = sb("std", [P, QT])
        rstd = sb("rstd", [P, QT])
        deg_mix = sb("deg_mix", [P, QT])
        deg_safe = sb("deg_safe", [P, QT])
        deg_some = sb("deg_some", [P, QT])
        deg_rec = sb("deg_rec", [P, QT])
        inv_diff = sb("inv_diff", [P, QT])
        row_sum = sb("row_sum", [P, JT])
        deg = sb("deg", [P, 3, JT])
        positive = sb("positive", [P, 2, JT])
        other = sb("other", [P, 2, JT])
        inv_deg = sb("inv_deg", [P, 3, JT])
        eps_t = sb("eps_t", [P, 1])
        ones = sb("ones", [P, 1])
        alpha_t = sb("alpha_t", [P, 1])
        one_less = sb("one_less", [P, 1])
        ident = sb("ident", [P, P])
        w = {name: sb("w_" + name, [P, P]) for name in mats}
        row_bias = {name: sb("rb_" + name, [P, P]) for name in rows}
        col_bias = {name: sb("cb_" + name, [P, 1]) for name in cols}

        ps_main = [psum(f"ps_main{i}", [P, CH]) for i in range(2)]
        ps_part = [psum(f"ps_part{i}", [P, CH]) for i in range(2)]
        ps_hid1 = psum("ps_hid1", [P, CH])
        ps_hid2 = psum("ps_hid2", [P, CH])
        ps_rows = psum("ps_rows", [P, CH])
        ps_deg = psum("ps_deg", [P, QT])

        x_landed = [sem(f"x_landed{g}") for g in range(NG)]
        consts_in = sem("consts_in")
        raw_in = [sem(f"raw_in{i}") for i in range(RING)]
        act_groups = sem("act_groups")
        dve_groups = sem("dve_groups")
        pe_groups = sem("pe_groups")
        set_up = sem("set_up")
        agg_copied = sem("agg_copied")
        part_copied = sem("part_copied")
        agg_added = sem("agg_added")
        rows_taken = sem("rows_taken")
        turned = sem("turned")
        turn_mixed = sem("turn_mixed")
        turn_copied = sem("turn_copied")
        hid1_done = sem("hid1_done")
        lin1_done = sem("lin1_done")
        hid1_copied = sem("hid1_copied")
        hid2_done = sem("hid2_done")
        lin2_done = sem("lin2_done")
        hid2_copied = sem("hid2_copied")
        rows_done = sem("rows_done")
        rows_read = sem("rows_read")
        folded = sem("folded")
        deg_step = sem("deg_step")
        lrelu_done = sem("lrelu_done")
        mlp_hi_done = sem("mlp_hi_done")
        pre_done = sem("pre_done")
        stats_done = sem("stats_done")
        moment_step = sem("moment_step")
        moments_done = sem("moments_done")
        std_done = sem("std_done")
        rstd_done = sem("rstd_done")
        norm_done = sem("norm_done")
        x_hi_done = sem("x_hi_done")
        x_done = sem("x_done")
        prep = sem("prep")
        stored = sem("stored")

        def source(p):
            return [None, 0, 1, 0, 1, 0, 1, 0, 0][p]

        def target(p):
            return [0, 1, 0, 1, 0, 1, 0][p]

        def norm_index(p, e):
            return e - NCH * p + NCH * NORMED[p]

        def chunk(t, c):
            h, b = c
            return t[:, :].rearrange("p (h b n) -> p h b n", b=2, n=CH)[:, h, b, :]

        def per_row(t, c, q):
            h, b = c
            return t.rearrange("p (h b q) -> p h b q", b=2, q=QT)[:, h, b, q:q + 1]

        def tile(t, q):
            return t[:, q * P:(q + 1) * P]

        def wait_landed(eng, slot, n):
            h, t = slot.c[0], slot.t0 + n
            if isinstance(t, int):
                eng.wait_ge(raw_in[t % RING], 16 * (t // RING + 1))
            else:
                t = FIRST_LOAD[slot.p] + NG * slot.c[1] + n
                eng.wait_ge(raw_in[t % RING], 16 * (t // RING + 1) + 16 * (2 * NG // RING) * h)

        def place(slot, n, buffers):
            t = slot.t0 if isinstance(slot.t0, int) else FIRST_LOAD[slot.p] + NG * slot.c[1]
            return (t + n) % buffers

        def wait_constants(eng, slot):
            if slot.e == 1:
                eng.wait_ge(consts_in, n_const)
                for g in range(NG):
                    eng.wait_ge(x_landed[g], 16)

        def wait_agg(eng, slot, back=0):
            if isinstance(slot.e, int):
                p, k = divmod(slot.e - back, NCH)
            else:
                p, k = slot.p, slot.e - NCH * slot.p - back
            if p in FOLLOWS:
                eng.wait_ge(agg_added, NCH * FOLLOWS[p] + k + 1)
            else:
                eng.wait_ge(agg_copied, NCH * (p - sum(f < p for f in FOLLOWS)) + k + 1)

        block = ctx.enter_context(nc.Block())

        @block.sync
        def _(sp):
            small = [(w[k], mats[k]) for k in mats] + [(ident, ident_d)]
            small += [(col_bias[k], cols[k].rearrange("(p a) -> p a", a=1)) for k in cols]
            small += [(row_bias[k], rows[k].rearrange("(a f) -> a f", a=1).to_broadcast([P, P])) for k in rows]
            small += [(alpha_t, alpha.rearrange("(a f) -> a f", a=1).to_broadcast([P, 1]))]

            for p in range(NPROD):
                blocks = (a_blocks if p == NPROD - 1 else at_blocks).rearrange("(h b) g p n -> h b g p n", b=2)
                for slot, _ in chunks(sp, p):
                    for n, g in enumerate(slot.groups):
                        t = slot.t0 + n
                        if not is_first(t, RING):
                            sp.wait_ge(dve_groups, t - RING + 1)
                            if p == 0 or is_first(t, FIRST_LOAD[1] + RING):
                                sp.wait_ge(act_groups, t - RING + 1)
                                sp.wait_ge(pe_groups, t - RING + 1)
                        k = place(slot, n, RING)
                        if is_first(t, NG):
                            own = slice(t * GJ * P, (t + 1) * GJ * P)
                            sp.dma_start(x_in[:, own], x[:, own]).then_inc(x_landed[t], 16)
                        sp.dma_start(raw[:, k, :], blocks[slot.c[0], slot.c[1], g]).then_inc(raw_in[k], 16)
                        if isinstance(t, int) and t == RING - 1:
                            for dst, src in small:
                                sp.dma_start(dst[:, :], src).then_inc(consts_in, 16)

        n_const = 16 * (1 + len(mats) + len(cols) + len(rows) + 1)

        @block.scalar
        def _(act):
            def group(slot, n):
                h, b = slot.c
                t = slot.t0 + n
                loaded = raw[:, place(slot, n, RING), :]
                wait_landed(act, slot, n)
                if slot.p == 0:
                    if not is_first(t):
                        act.wait_ge(act_groups, t)
                    part = col_part[:, :].rearrange("p (h b j) -> p h b j", b=2, j=JT)
                    for j in range(GJ):
                        last = nc.scalar.activation(junk[:, j, :], loaded[:, j * CH:(j + 1) * CH], ACT.Copy,
                                                    accum_out=part[:, h, b, GJ * n + j:GJ * n + j + 1])
                    last.then_inc(act_groups, 1)
                else:
                    if not is_first(t, FIRST_LOAD[1] + HALF):
                        act.wait_ge(pe_groups, t - HALF + 1)
                    nc.scalar.copy(a_hi[:, place(slot, n, HALF), :], loaded).then_inc(act_groups, 1)

            def epilogue(slot, g):
                p, c, e, kind = slot.p, slot.c, slot.e, KIND[slot.p]
                at = STEPS[kind]
                n = e - NCH * 2
                if g == 0 and kind in (DIFF, MEAN):
                    if not is_first(e):
                        act.wait_ge(turned, e)
                    nc.scalar.copy(rows_in[:, :], chunk(x_in if kind == DIFF else x_res, c)).then_inc(rows_taken, 1)
                if g == at["agg"] and p not in FOLLOWS:
                    act.wait_ge(pe_groups, slot.t0 + len(slot.groups))
                    if kind in (MLP, MLP_NORM) and n > 0:
                        act.wait_ge(hid1_done, n)
                    elif not is_first(e):
                        act.wait_ge(rows_done, e)
                    bank = ps_main[c[1] if not isinstance(e, int) else e % 2]
                    if kind == DIFF:
                        nc.scalar.activation(agg[:, :], bank[:, :], ACT.Copy, scale=alpha_t[:, :]).then_inc(agg_copied, 1)
                    else:
                        nc.scalar.copy(agg[:, :], bank[:, :]).then_inc(agg_copied, 1)
                    if p in LEADS and number(slot):
                        if LEADS[p]:
                            act.wait_ge(agg_added, NCH * LEADS[p])
                        nc.scalar.copy(partial[:, number(slot) - 1, :],
                                       ps_part[number(slot) % 2][:, :]).then_inc(part_copied, 1)
                    if kind == MEAN:
                        act.wait_ge(turned, e + 1)
                        nc.scalar.copy(hid1[:, :], ps_hid1[:, :]).then_inc(turn_copied, 1)
                if g == at.get("lin1"):
                    bias = col_bias["uv_b1" if p % 2 == 0 else "vu_b1"]
                    act.wait_ge(hid1_done, n + 1)
                    if n > 0:
                        act.wait_ge(hid1_copied, n)
                    nc.scalar.activation(lin1[:, :], ps_hid1[:, :], ACT.Identity, bias=bias[:, :]).then_inc(lin1_done, 1)
                if g == at.get("lin2"):
                    bias = col_bias["uv_b2" if p % 2 == 0 else "vu_b2"]
                    act.wait_ge(hid2_done, n + 1)
                    if n > 0:
                        act.wait_ge(hid2_copied, n)
                    nc.scalar.activation(lin2[:, :], ps_hid2[:, :], ACT.Identity, bias=bias[:, :]).then_inc(lin2_done, 1)
                if g == at.get("hi") and kind == MLP:
                    act.wait_ge(lrelu_done, n + 1)
                    nc.scalar.copy(chunk(x_hi[target(p)], c), rows_out[:, :]).then_inc(mlp_hi_done, 1)
                if p in NORMED:
                    k = norm_index(p, e)
                    if g == at["std"]:
                        act.wait_ge(moments_done, k + 1)
                        nc.scalar.activation(std[:, :], var[:, :], ACT.Sqrt, bias=eps_t[:, :]).then_inc(std_done, 1)
                    if g == at["hi"] and kind != OUTMSG:
                        act.wait_ge(norm_done, k + 1)
                        nc.scalar.copy(chunk(x_hi[target(p)], c), rows_out[:, :])
                        nc.scalar.copy(chunk(x_res, c), rows_out[:, :]).then_inc(x_hi_done, 1)
                    if g == at["hi"] and kind == OUTMSG:
                        act.wait_ge(norm_done, k + 1)
                        dst = out.rearrange("(h b q p) f -> h b p q f", b=2, q=QT, p=P)[c[0], c[1]]
                        act.dma_start(dst, rows_out[:, :].rearrange("p (q f) -> p q f", q=QT)).then_inc(stored, 16)

            for p in range(NPROD):
                for slot, steps in chunks(act, p):
                    if is_first(slot.e, 2):
                        wait_constants(act, slot)
                    for n in range(len(slot.groups)):
                        for step in steps[n]:
                            epilogue(*step)
                        group(slot, n)
            for step in last_steps():
                epilogue(*step)
            act.wait_ge(stored, 16 * NCH)

        @block.vector
        def _(dve):
            def group(slot, n):
                t = slot.t0 + n
                loaded = raw[:, place(slot, n, RING), :]
                if slot.p == 0:
                    wait_landed(dve, slot, n)
                    if n == 0:
                        if not is_first(t):
                            dve.wait_ge(folded, slot.e)
                        nc.vector.tensor_copy(acc[:, :], loaded).then_inc(dve_groups, 1)
                    else:
                        dve.wait_ge(dve_groups, t)
                        nc.vector.tensor_tensor(acc[:, :], acc[:, :], loaded, ALU.add).then_inc(dve_groups, 1)
                    if n == NG - 1:
                        dve.wait_ge(dve_groups, t + 1)
                        nc.vector.tensor_reduce(fold[:, :], acc[:, :].rearrange("p (j n) -> p n j", j=GJ),
                                                AX.X, ALU.add).then_inc(folded, 1)
                else:
                    if not is_first(t, FIRST_LOAD[1] + HALF):
                        dve.wait_ge(pe_groups, t - HALF + 1)
                    dve.wait_ge(act_groups, t + 1)
                    k = place(slot, n, HALF)
                    nc.vector.tensor_tensor(a_lo[:, k, :], loaded, a_hi[:, k, :].bitcast(F32),
                                            ALU.subtract).then_inc(dve_groups, 1)

            def epilogue(slot, g):
                p, c, e, kind = slot.p, slot.c, slot.e, KIND[slot.p]
                at = STEPS[kind]
                normed = p in NORMED
                k = norm_index(p, e) if normed else None
                n = e - NCH * 2
                if g == at["agg"] and p in FOLLOWS:
                    dve.wait_ge(pe_groups, slot.t0 + len(slot.groups))
                    if kind == MLP:
                        dve.wait_ge(hid1_done, n)
                    else:
                        dve.wait_ge(rows_done, e)
                    if number(slot):
                        dve.wait_ge(part_copied, (NCH - 1) * FOLLOWS[p] + number(slot))
                        nc.vector.tensor_tensor(agg[:, :], ps_main[e % 2][:, :], partial[:, number(slot) - 1, :],
                                                ALU.add).then_inc(agg_added, 1)
                    else:
                        nc.vector.tensor_copy(agg[:, :], ps_main[e % 2][:, :]).then_inc(agg_added, 1)
                if g == at.get("mix"):
                    wait_agg(dve, slot)
                    dve.wait_ge(turned, e + 1)
                    if not is_first(e):
                        dve.wait_ge(rows_done, e)
                    nc.vector.scalar_tensor_tensor(hid1[:, :], ps_hid1[:, :], one_less[:, :], agg[:, :],
                                                   ALU.mult, ALU.add).then_inc(turn_mixed, 1)
                if g == at.get("act1"):
                    dve.wait_ge(lin1_done, n + 1)
                    if n > 0:
                        dve.wait_ge(hid2_done, n)
                    else:
                        dve.wait_ge(rows_done, e)
                    nc.vector.scalar_tensor_tensor(hid1[:, :], lin1[:, :], SLOPE, lin1[:, :],
                                                   ALU.mult, ALU.max).then_inc(hid1_copied, 1)
                if g == at.get("act2"):
                    dve.wait_ge(lin2_done, n + 1)
                    dve.wait_ge(rows_done, e)
                    nc.vector.scalar_tensor_tensor(hid2[:, :], lin2[:, :], SLOPE, lin2[:, :],
                                                   ALU.mult, ALU.max).then_inc(hid2_copied, 1)
                if g == at["sums"]:
                    dve.wait_ge(rows_done, e + 1)
                    if kind == DIFF:
                        nc.vector.tensor_copy(per_row4(row_sum[:, :], c), ps_deg[:, :])
                        nc.vector.tensor_scalar(deg_mix[:, :], ps_deg[:, :], alpha_t[:, :], one_less[:, :],
                                                ALU.mult, ALU.add).then_inc(deg_step, 1)
                        dve.wait_ge(deg_step, 4 * e + 1)
                        nc.vector.scalar_tensor_tensor(deg_safe[:, :], deg_mix[:, :], 0.0, deg_mix[:, :],
                                                       ALU.is_equal, ALU.add)
                        nc.vector.tensor_scalar(deg_some[:, :], deg_mix[:, :], 0.0, None,
                                                ALU.not_equal).then_inc(deg_step, 1)
                        dve.wait_ge(deg_step, 4 * e + 2)
                        nc.vector.reciprocal(deg_rec[:, :], deg_safe[:, :]).then_inc(deg_step, 1)
                        dve.wait_ge(deg_step, 4 * e + 3)
                        nc.vector.tensor_tensor(inv_diff[:, :], deg_rec[:, :], deg_some[:, :],
                                                ALU.mult).then_inc(deg_step, 1)
                        dve.wait_ge(deg_step, 4 * e + 4)
                        for q in range(QT):
                            last = nc.vector.scalar_tensor_tensor(tile(biased, q), tile(ps_rows, q), inv_diff[:, q:q + 1],
                                                                  row_bias["b"][:, :], ALU.mult, ALU.add)
                        last.then_inc(rows_read, 1)
                        dve.wait_ge(rows_read, e + 1)
                        nc.vector.scalar_tensor_tensor(pre[:, :], biased[:, :], 0.0, chunk(x_in, c),
                                                       ALU.max, ALU.add).then_inc(pre_done, 1)
                    elif kind == MEAN:
                        for q in range(QT):
                            last = nc.vector.scalar_tensor_tensor(tile(biased, q), tile(ps_rows, q), per_row(inv_deg[:, 0, :], c, q),
                                                                  chunk_tile(x_res, c, q), ALU.mult, ALU.add)
                        last.then_inc(rows_read, 1)
                        dve.wait_ge(rows_read, e + 1)
                        nc.vector.tensor_tensor(pre[:, :], biased[:, :], ps_hid2[:, :], ALU.add).then_inc(pre_done, 1)
                    elif kind in (MLP, MLP_NORM):
                        b3 = row_bias["uv_b3" if p % 2 == 0 else "vu_b3"]
                        nc.vector.tensor_tensor(biased[:, :].rearrange("p (q f) -> p q f", q=QT),
                                                ps_rows[:, :].rearrange("p (q f) -> p q f", q=QT),
                                                b3[:, :].rearrange("p (a f) -> p a f", a=1).to_broadcast([P, QT, P]),
                                                ALU.add).then_inc(rows_read, 1)
                        dve.wait_ge(rows_read, e + 1)
                        if kind == MLP and n > 0:
                            dve.wait_ge(x_done, e)
                        new = rows_out if kind == MLP else lrelu3
                        nc.vector.scalar_tensor_tensor(new[:, :], biased[:, :], SLOPE, biased[:, :],
                                                       ALU.mult, ALU.max).then_inc(lrelu_done, 1)
                    elif kind == INMSG:
                        for q in range(QT):
                            r = chunk_tile(x_res, c, q)
                            last = nc.vector.scalar_tensor_tensor(r, tile(ps_rows, q), per_row(inv_deg[:, 1, :], c, q),
                                                                  r, ALU.mult, ALU.add)
                        last.then_inc(rows_read, 1)
                    else:
                        for q in range(QT):
                            last = nc.vector.scalar_tensor_tensor(tile(pre, q), tile(ps_rows, q), per_row(inv_deg[:, 2, :], c, q),
                                                                  chunk_tile(x_res, c, q), ALU.mult, ALU.add)
                        last.then_inc(rows_read, 1)
                if kind == MLP and g == at["lo"]:
                    dve.wait_ge(mlp_hi_done, e - 2 * NCH + 1)
                    nc.vector.tensor_tensor(chunk(x_lo[target(p)], c), rows_out[:, :],
                                            chunk(x_hi[target(p)], c).bitcast(F32), ALU.subtract).then_inc(x_done, 1)
                if kind == MLP_NORM and g == at["stats"]:
                    dve.wait_ge(lrelu_done, e - 2 * NCH + 1)
                    dve.wait_ge(norm_done, k)
                    nc.vector.tensor_tensor(pre[:, :], lrelu3[:, :], chunk(x_res, c), ALU.add).then_inc(pre_done, 1)
                if not normed:
                    return
                if g == at["stats"]:
                    if kind == OUTMSG:
                        dve.wait_ge(rows_read, e + 1)
                    else:
                        dve.wait_ge(pre_done, k + 1)
                    for q in range(QT):
                        last = nc.vector.bn_stats(stats[:, q, :], tile(pre, q))
                    last.then_inc(stats_done, 1)
                    dve.wait_ge(stats_done, k + 1)
                    nc.vector.tensor_tensor(mean2[:, :], stats[:, :, 1], stats[:, :, 4], ALU.add)
                    nc.vector.tensor_tensor(gap[:, :], stats[:, :, 1], stats[:, :, 4], ALU.subtract)
                    nc.vector.tensor_tensor(squares[:, :], stats[:, :, 2], stats[:, :, 5],
                                            ALU.add).then_inc(moment_step, 1)
                    dve.wait_ge(moment_step, 2 * k + 1)
                    nc.vector.tensor_scalar(mean[:, :], mean2[:, :], 0.5, None, ALU.mult)
                    nc.vector.scalar_tensor_tensor(gap2[:, :], gap[:, :], 0.25, gap[:, :],
                                                   ALU.mult, ALU.mult).then_inc(moment_step, 1)
                    dve.wait_ge(moment_step, 2 * k + 2)
                    nc.vector.scalar_tensor_tensor(var[:, :], squares[:, :], 1.0 / P, gap2[:, :],
                                                   ALU.mult, ALU.add).then_inc(moments_done, 1)
                if g == at["norm"]:
                    dve.wait_ge(std_done, k + 1)
                    nc.vector.reciprocal(rstd[:, :], std[:, :]).then_inc(rstd_done, 1)
                    dve.wait_ge(rstd_done, k + 1)
                    if kind == OUTMSG and not (isinstance(e, int) and e == NCH * p):
                        dve.wait_ge(stored, 16 * (e - NCH * p))
                    for q in range(QT):
                        last = nc.vector.tensor_scalar(tile(rows_out, q), tile(pre, q), mean[:, q:q + 1], rstd[:, q:q + 1],
                                                       ALU.subtract, ALU.mult)
                    last.then_inc(norm_done, 1)
                if g == at.get("lo"):
                    dve.wait_ge(x_hi_done, k + 1)
                    nc.vector.tensor_tensor(chunk(x_lo[target(p)], c), rows_out[:, :],
                                            chunk(x_hi[target(p)], c).bitcast(F32), ALU.subtract).then_inc(x_done, 1)

            def per_row4(t, c):
                return t.rearrange("p (h b q) -> p h b q", b=2, q=QT)[:, c[0], c[1], :]

            def chunk_tile(t, c, q):
                return t[:, :].rearrange("p (h b q f) -> p h b q f", b=2, q=QT, f=P)[:, c[0], c[1], q, :]

            def degrees():
                dve.wait_ge(act_groups, NCH * NG)
                dve.wait_ge(rows_read, NCH)
                nc.vector.tensor_reduce(deg[:, 2, :], col_part[:, :].rearrange("p (c j) -> p j c", c=NCH), AX.X, ALU.add)
                nc.vector.tensor_copy(deg[:, 1, :], row_sum[:, :])
                nc.vector.tensor_scalar(deg[:, 0, :], row_sum[:, :], 1.0, None, ALU.max).then_inc(prep, 1)
                dve.wait_ge(prep, 1)
                nc.vector.tensor_scalar(positive[:, :, :], deg[:, 1:3, :], 0.0, None, ALU.is_gt)
                nc.vector.tensor_scalar(other[:, :, :], deg[:, 1:3, :], 0.0, None, ALU.is_le).then_inc(prep, 1)
                dve.wait_ge(prep, 2)
                nc.vector.tensor_tensor(deg[:, 1:3, :], deg[:, 1:3, :], positive[:, :, :], ALU.mult).then_inc(prep, 1)
                dve.wait_ge(prep, 3)
                nc.vector.tensor_tensor(deg[:, 1:3, :], deg[:, 1:3, :], other[:, :, :], ALU.add).then_inc(prep, 1)
                dve.wait_ge(prep, 4)
                nc.vector.reciprocal(inv_deg[:, :, :], deg[:, :, :]).then_inc(prep, 1)
                dve.wait_ge(prep, 5)

            nc.vector.memset(eps_t[:, :], EPS)
            nc.vector.memset(ones[:, :], 1.0)
            for p in range(NPROD):
                for slot, steps in chunks(dve, p):
                    if is_first(slot.e, 2):
                        wait_constants(dve, slot)
                        if slot.e:
                            nc.vector.tensor_scalar(one_less[:, :], alpha_t[:, :], -1.0, 1.0,
                                                    ALU.mult, ALU.add).then_inc(set_up, 1)
                            dve.wait_ge(set_up, 1)
                    for n in range(len(slot.groups)):
                        for step in steps[n]:
                            epilogue(*step)
                        group(slot, n)
                    if is_first(slot.e, NCH + 1) and not is_first(slot.e, NCH):
                        degrees()
            for step in last_steps():
                epilogue(*step)

        @block.tensor
        def _(pe):
            def split_product(bank, p, g, k, first, final):
                hi, lo = x_hi[source(p)], x_lo[source(p)]
                for j in range(GJ):
                    block_hi = a_hi[:, k, j * CH:(j + 1) * CH]
                    block_lo = a_lo[:, k, j * CH:(j + 1) * CH]
                    jt = GJ * g + j
                    nc.tensor.matmul(bank[:, :], tile(hi, jt), block_hi, start=first and j == 0, stop=False)
                    nc.tensor.matmul(bank[:, :], tile(hi, jt), block_lo, start=False, stop=False)
                    last = nc.tensor.matmul(bank[:, :], tile(lo, jt), block_hi, start=False, stop=final and j == GJ - 1)
                return last

            def group(slot, n):
                p, e, t, g = slot.p, slot.e, slot.t0 + n, slot.groups[n]
                bank = ps_main[slot.c[1] if not isinstance(e, int) else e % 2]
                if n == 0 and not is_first(e, 2):
                    wait_agg(pe, slot, back=2)
                if p == 0:
                    wait_landed(pe, slot, n)
                    if is_first(e):
                        pe.wait_ge(x_landed[n], 16)
                    k = place(slot, n, RING)
                    for j in range(GJ):
                        jt = GJ * g + j
                        last = nc.tensor.matmul(bank[:, :], tile(x_in, jt), raw[:, k, j * CH:(j + 1) * CH],
                                                start=jt == 0, stop=jt == JT - 1)
                else:
                    if p < NPROD - 1 and isinstance(e, int) and e == NCH * p:
                        pe.wait_ge(x_done, NCH * (p - 1) + order_of(p - 1).index(g) + 1)
                    pe.wait_ge(dve_groups, t + 1)
                    k = place(slot, n, HALF)
                    last = split_product(bank, p, g, k, n == 0, n == len(slot.groups) - 1)
                    if p in LEADS and g < number(slot):
                        i, pair = number(slot), LEADS[p]
                        if g == 0:
                            if (NCH - 1) * pair + max(i - 2, 0) > 0:
                                pe.wait_ge(part_copied, (NCH - 1) * pair + max(i - 2, 0))
                        if g == i - 1:
                            pe.wait_ge(x_done, e)
                        last = split_product(ps_part[i % 2], p + 1, g, k, g == 0, g == i - 1)
                last.then_inc(pe_groups, 1)

            def by_rows(ps, lhs, weight):
                for q in range(QT):
                    last = nc.tensor.matmul(tile(ps, q), tile(lhs, q), weight[:, :], start=True, stop=True)
                return last

            def epilogue(slot, g):
                p, c, e, kind = slot.p, slot.c, slot.e, KIND[slot.p]
                at = STEPS[kind]
                n = e - NCH * 2
                tag = "uv" if p % 2 == 0 else "vu"
                if g == at.get("turn"):
                    pe.wait_ge(rows_taken, e + 1)
                    if not is_first(e):
                        if kind == DIFF or is_first(e, NCH + 1):
                            pe.wait_ge(turn_mixed, e)
                        else:
                            pe.wait_ge(turn_copied, e - NCH)
                    for q in range(QT):
                        last = nc.tensor.transpose(tile(ps_hid1, q), tile(rows_in, q), ident[:, :])
                    last.then_inc(turned, 1)
                if g == at.get("hid1"):
                    wait_agg(pe, slot)
                    nc.tensor.matmul(ps_hid1[:, :], w[tag + "_W1"][:, :], agg[:, :], start=True, stop=True).then_inc(hid1_done, 1)
                if g == at.get("hid2"):
                    pe.wait_ge(hid1_copied, n + 1)
                    if p == 2 and isinstance(e, int) and e == NCH * p:
                        pe.wait_ge(pre_done, e)
                    nc.tensor.matmul(ps_hid2[:, :], w[tag + "_W2"][:, :], hid1[:, :], start=True, stop=True).then_inc(hid2_done, 1)
                if g == at["rows"]:
                    if not is_first(e):
                        pe.wait_ge(rows_read, e)
                    if kind not in (DIFF, MLP, MLP_NORM):
                        wait_agg(pe, slot)
                    if kind == DIFF:
                        pe.wait_ge(turn_mixed, e + 1)
                        pe.wait_ge(folded, e + 1)
                        by_rows(ps_rows, hid1, w["W_t"])
                        for q in range(QT):
                            last = nc.tensor.matmul(ps_deg[:, q:q + 1], tile(fold, q), ones[:, :], start=True, stop=True)
                    elif kind == MEAN:
                        pe.wait_ge(turn_copied, e - NCH + 1)
                        pe.wait_ge(pre_done, e)
                        by_rows(ps_rows, agg, w["W_neigh"])
                        last = by_rows(ps_hid2, hid1, w["W_self"])
                    elif kind in (MLP, MLP_NORM):
                        pe.wait_ge(hid2_copied, n + 1)
                        last = by_rows(ps_rows, hid2, w[tag + "_W3"])
                    else:
                        last = by_rows(ps_rows, agg, w["W_in" if kind == INMSG else "W_out"])
                    last.then_inc(rows_done, 1)

            for p in range(NPROD):
                for slot, steps in chunks(pe, p):
                    if is_first(slot.e, 2):
                        wait_constants(pe, slot)
                    for n in range(len(slot.groups)):
                        for step in steps[n]:
                            epilogue(*step)
                        group(slot, n)
            for step in last_steps():
                epilogue(*step)


MATS = {"W_t": ("L0_gnn_W", True), "W_self": ("L1_gnn_W_self", False), "W_neigh": ("L1_gnn_W_neigh", False),
        "W_in": ("L3_gnn_W_in", False), "W_out": ("L3_gnn_W_out", False)}
MATS |= {f"{t}_W{i}": (f"L2_gnn_{t}_W{i}", False) for t in ("uv", "vu") for i in (1, 2, 3)}
ROWS = {"b": "L0_gnn_b", "uv_b3": "L2_gnn_uv_b3", "vu_b3": "L2_gnn_vu_b3"}
COLS = {f"{t}_b{i}": f"L2_gnn_{t}_b{i}" for t in ("uv", "vu") for i in (1, 2)}


def blocks(a, np):
    a = a.reshape(NG, GJ, P, NCH, CH).transpose(3, 0, 2, 1, 4)
    return np.ascontiguousarray(a).reshape(NCH, NG, P, GW)


def kernel(**inputs):
    import numpy as np
    import concourse.bacc as bacc
    from concourse.bass_utils import run_bass_kernel_spmd as run

    nc = bacc.Bacc("TRN2", target_bir_lowering=False, num_devices=1, dynamic_dma_scratch_size=512)
    arrays = {}

    def give(name, a):
        name = "in_" + name
        arrays[name] = np.ascontiguousarray(a)
        return nc.dram_tensor(name, arrays[name].shape, mybir.dt.from_np(arrays[name].dtype), kind="ExternalInput").ap()

    adj = np.asarray(inputs["adj"])
    x = np.asarray(inputs["x"])
    x_d = give("x", x.reshape(JT, P, P).transpose(1, 0, 2).reshape(P, JT * P))
    at_d = give("at", blocks(adj.T, np))
    a_d = give("a", blocks(adj, np))
    mats = {k: give(k, np.asarray(inputs[s]).T if t else np.asarray(inputs[s])) for k, (s, t) in MATS.items()}
    rows = {k: give(k, np.asarray(inputs[s])) for k, s in ROWS.items()}
    cols = {k: give(k, np.asarray(inputs[s])) for k, s in COLS.items()}
    alpha = give("alpha", np.asarray(inputs["L0_gnn_alpha"]))
    ident = give("ident", np.eye(P, dtype=np.float32))
    out = nc.dram_tensor("out", (N, P), F32, kind="ExternalOutput").ap()
    adj_resnorm(nc, x_d, at_d, a_d, mats, rows, cols, alpha, ident, out)
    r = run(nc, [arrays], core_ids=[0])
    return r.results[0]["out"]
```
